# Optimizing a Trainium2 kernel written in Bass

```python
import numpy as np
import jax
import jax.numpy as jnp

def _softmax(x, axis=-1):
    return jax.nn.softmax(x, axis=axis)

def _gelu(x):
    return jax.nn.gelu(x, approximate=True)

def _silu(x):
    return jax.nn.silu(x)

def _sigmoid(x):
    return jax.nn.sigmoid(x)

def _layernorm(x, axis=-1, eps=1e-05):
    m = jnp.mean(x, axis=axis, keepdims=True)
    v = jnp.var(x, axis=axis, keepdims=True)
    return (x - m) / jnp.sqrt(v + eps)

def _scatter_add(tgt, idx, src, axis=0):
    return tgt.at[idx].add(src)

def _segment_sum(src, seg, n):
    return jax.ops.segment_sum(src, seg, n)
kernel_name = 'mk_rec_standalone_d1_rec_r8_aebe8f'

def setup_inputs(seed: int=0):
    np.random.seed(seed)
    _w = jnp.asarray

    def _rec_inputs():
        import jax
        import jax.numpy as jnp
        _rk = jax.random.key(seed)
        r_w_features = jax.random.uniform(jax.random.fold_in(_rk, 1), (1024, 5120), jnp.float32, 0.0, 1)
        r_b_features = jax.random.uniform(jax.random.fold_in(_rk, 2), (1024, 5120), jnp.float32, 0.0, 1)
        r_white_to_move = jax.random.uniform(jax.random.fold_in(_rk, 3), (1024, 1), jnp.float32, 0.0, 0.999707)
        return (r_w_features, r_b_features, r_white_to_move)
    r_w_features, r_b_features, r_white_to_move = _rec_inputs()

    def _L0_rec_setup():
        import jax, jax.numpy as jnp
        import numpy as np
        INPUT_LAYER_SIZE = 5120
        L1, L2, L3 = (256, 32, 32)
        key = jax.random.key(seed)
        ks = jax.random.split(key, 12)
        B = 512
        w_features = jax.random.uniform(ks[0], (B, INPUT_LAYER_SIZE), dtype=jnp.float32)
        b_features = jax.random.uniform(ks[1], (B, INPUT_LAYER_SIZE), dtype=jnp.float32)
        white_to_move = jax.random.uniform(ks[2], (B, 1), dtype=jnp.float32)
        s_in = 1.0 / np.sqrt(INPUT_LAYER_SIZE)
        s1 = 1.0 / np.sqrt(2 * L1)
        s2 = 1.0 / np.sqrt(L2)
        s3 = 1.0 / np.sqrt(L3)
        W_in = jax.random.uniform(ks[3], (L1, INPUT_LAYER_SIZE), jnp.float32, -s_in, s_in)
        b_in = jax.random.uniform(ks[4], (L1,), jnp.float32, -s_in, s_in)
        W1 = jax.random.uniform(ks[5], (L2, 2 * L1), jnp.float32, -s1, s1)
        b1 = jax.random.uniform(ks[6], (L2,), jnp.float32, -s1, s1)
        W2 = jax.random.uniform(ks[7], (L3, L2), jnp.float32, -s2, s2)
        b2 = jax.random.uniform(ks[8], (L3,), jnp.float32, -s2, s2)
        W3 = jax.random.uniform(ks[9], (1, L3), jnp.float32, -s3, s3)
        b3 = jax.random.uniform(ks[10], (1,), jnp.float32, -s3, s3)
        return {'w_features': w_features, 'b_features': b_features, 'white_to_move': white_to_move, 'W_in': W_in, 'b_in': b_in, 'W1': W1, 'b1': b1, 'W2': W2, 'b2': b2, 'W3': W3, 'b3': b3}
    _L0_rec_all = _L0_rec_setup()
    _L0_rec_in = {k: v for k, v in _L0_rec_all.items() if k in ('W_in', 'b_in', 'W1', 'b1', 'W2', 'b2', 'W3', 'b3')}
    del _L0_rec_all
    return {'r_w_features': r_w_features, 'r_b_features': r_b_features, 'r_white_to_move': r_white_to_move, 'L0_rec_W_in': _L0_rec_in['W_in'], 'L0_rec_b_in': _L0_rec_in['b_in'], 'L0_rec_W1': _L0_rec_in['W1'], 'L0_rec_b1': _L0_rec_in['b1'], 'L0_rec_W2': _L0_rec_in['W2'], 'L0_rec_b2': _L0_rec_in['b2'], 'L0_rec_W3': _L0_rec_in['W3'], 'L0_rec_b3': _L0_rec_in['b3']}

def reference(r_w_features, r_b_features, r_white_to_move, L0_rec_W_in, L0_rec_b_in, L0_rec_W1, L0_rec_b1, L0_rec_W2, L0_rec_b2, L0_rec_W3, L0_rec_b3):
    import jax
    import jax.numpy as jnp

    def _L0_rec_ref(w_features, b_features, white_to_move, W_in, b_in, W1, b1, W2, b2, W3, b3):
        import jax, jax.numpy as jnp
        import numpy as np
        INPUT_LAYER_SIZE = 5120
        L1, L2, L3 = (256, 32, 32)
        white = w_features @ W_in.T + b_in
        black = b_features @ W_in.T + b_in
        wb = jnp.concatenate([white, black], axis=1)
        bw = jnp.concatenate([black, white], axis=1)
        accum = white_to_move * wb + (1.0 - white_to_move) * bw
        h1 = jnp.clip(accum, 0.0, 1.0)
        h2 = jnp.clip(h1 @ W1.T + b1, 0.0, 1.0)
        h3 = jnp.clip(h2 @ W2.T + b2, 0.0, 1.0)
        return h3 @ W3.T + b3
    y = _L0_rec_ref(r_w_features, r_b_features, r_white_to_move, L0_rec_W_in, L0_rec_b_in, L0_rec_W1, L0_rec_b1, L0_rec_W2, L0_rec_b2, L0_rec_W3, L0_rec_b3)
    return y

_drawn_inputs = setup_inputs


def setup_inputs(seed=0):
    import zlib

    import numpy as np

    out = dict(_drawn_inputs(seed))
    spreads = {}
    factors = {}
    for name, (base, spread) in spreads.items():
        noise = np.random.default_rng([zlib.crc32(name.encode()), seed]).standard_normal(out[name].shape)
        drawn = base * np.exp(spread * noise) if base else spread * noise
        out[name] = jnp.asarray(drawn.astype(out[name].dtype))
    for name, factor in factors.items():
        out[name] = (out[name] * factor).astype(out[name].dtype)
    return out
```

```python
import numpy as np
import concourse.bass as bass
import concourse.mybir as mybir
from concourse.alu_op_type import AluOpType as ALU

ROWS = 1024
FEATURES = 5120
HIDDEN = 256
NARROW = 32
P = 128
K_TILES = FEATURES // P
M_TILES = HIDDEN // P
QUARTERS = 4
Q_ROWS = ROWS // QUARTERS
COLS = 2 * Q_ROWS
GROUP = 2
GROUPS = K_TILES // GROUP
SLOTS = 4
TURNS = GROUPS // SLOTS
ALL_TURNS = TURNS * QUARTERS
MLP_CHUNKS = 2 * HIDDEN // P
LAYER1_AFTER, LAYER2_AFTER, LAYER3_AFTER = 8, 10, 12

W1_AT = 0
B_IN_AT = W1_AT + MLP_CHUNKS * NARROW
B1_AT = B_IN_AT + M_TILES
W2_AT = B1_AT + 1
W3_AT = W2_AT + P
SMALL_COLS = W3_AT + P


def nnue_program(nc, features, w_in, white_to_move, small, out):
    f32, f32r = mybir.dt.float32, mybir.dt.float32r
    ACT = mybir.ActivationFunctionType

    from contextlib import ExitStack
    with ExitStack() as ctx:
        def sb(name, shape, dt=f32):
            return ctx.enter_context(nc.sbuf_tensor(name, shape, dt))

        def sem(name):
            return ctx.enter_context(nc.semaphore(name))

        w_hi = sb("w_hi", [P, K_TILES * HIDDEN], f32r)
        w_lo = sb("w_lo", [P, K_TILES * HIDDEN], f32r)
        w_raw = sb("w_raw", [P, SLOTS, GROUP * HIDDEN])
        x_raw = sb("x_raw", [P, SLOTS, GROUP * COLS])
        x_hi = sb("x_hi", [P, SLOTS, GROUP * COLS], f32r)
        x_lo = sb("x_lo", [P, SLOTS, GROUP * COLS], f32r)
        params = sb("params", [P, SMALL_COLS])
        side = sb("side", [P, ROWS])
        colours = sb("colours", [P, M_TILES, COLS])
        swing = sb("swing", [P, M_TILES, Q_ROWS])
        h1 = sb("h1", [P, M_TILES, 2, Q_ROWS])
        h2 = sb("h2", [NARROW + 1, Q_ROWS])
        h3 = sb("h3", [NARROW + 1, Q_ROWS])
        scores = sb("scores", [1, ROWS])
        acc = ctx.enter_context(nc.psum_tensor("acc", [P, 2 * QUARTERS, 512], f32))
        layer1 = acc[0:NARROW, 0, 0:Q_ROWS]
        layer2 = acc[:, 0, Q_ROWS:2 * Q_ROWS]
        layer3 = acc[:, 1, 0:Q_ROWS]

        params_in = sem("params_in")
        side_in = sem("side_in")
        w_in_slot = [sem(f"w_in_slot{s}") for s in range(SLOTS)]
        x_in_slot = [sem(f"x_in_slot{s}") for s in range(SLOTS)]
        w_hi_ready = sem("w_hi_ready")
        w_lo_ready = sem("w_lo_ready")
        x_hi_ready = sem("x_hi_ready")
        x_lo_ready = sem("x_lo_ready")
        x_used = sem("x_used")
        first_acc_ready = sem("first_acc_ready")
        colours_ready = sem("colours_ready")
        swing_step = sem("swing_step")
        h1_ready = sem("h1_ready")
        ones_ready = sem("ones_ready")
        layer1_ready = sem("layer1_ready")
        relu1_ready = sem("relu1_ready")
        h2_ready = sem("h2_ready")
        layer2_ready = sem("layer2_ready")
        h3_ready = sem("h3_ready")
        layer3_ready = sem("layer3_ready")
        scores_ready = sem("scores_ready")
        out_done = sem("out_done")
        STEPS = 4

        block = ctx.enter_context(nc.Block())

        @block.sync
        def _(sp):
            def load_w(group, s):
                sp.dma_start(w_raw[:, s, :], w_in[:, bass.ds(group * (GROUP * HIDDEN), GROUP * HIDDEN)]
                             ).then_inc(w_in_slot[s], 16)

            def load_x(group, s):
                sp.dma_start(x_raw[:, s, :], features[bass.ds(group, 1), :, :].rearrange("a p n -> (a p) n")
                             ).then_inc(x_in_slot[s], 16)

            for s in range(SLOTS):
                load_w(s, s)
                load_x(s, s)
            with sp.Fori(1, TURNS) as turn:
                for s in range(SLOTS):
                    sp.wait_ge(w_lo_ready, (turn - 1) * SLOTS + s + 1)
                    load_w(turn * SLOTS + s, s)
                    sp.wait_ge(x_lo_ready, (turn - 1) * SLOTS + s + 1)
                    load_x(turn * SLOTS + s, s)
            with sp.Fori(TURNS, ALL_TURNS) as turn:
                for s in range(SLOTS):
                    sp.wait_ge(x_lo_ready, (turn - 1) * SLOTS + s + 1)
                    load_x(turn * SLOTS + s, s)
            sp.wait_ge(scores_ready, QUARTERS)
            sp.dma_start(out, scores[0:1, :]).then_inc(out_done, 16)
            sp.wait_ge(out_done, 16)

        @block.gpsimd
        def _(pool):
            pool.dma_start(params[:, :], small).then_inc(params_in, 16)
            pool.dma_start(side[:, :], white_to_move.to_broadcast([P, ROWS])).then_inc(side_in, 16)
            nc.gpsimd.memset(h2[NARROW:NARROW + 1, :], 1.0).then_inc(ones_ready, 1)
            nc.gpsimd.memset(h3[NARROW:NARROW + 1, :], 1.0).then_inc(ones_ready, 1)

        @block.scalar
        def _(act):
            def split_w(turn, s, group):
                act.wait_ge(w_in_slot[s], 16 * (turn + 1))
                nc.scalar.activation(w_hi[:, bass.ds(group * (GROUP * HIDDEN), GROUP * HIDDEN)],
                                     w_raw[:, s, :], ACT.Copy).then_inc(w_hi_ready, 1)

            def split_x(turn, s, group, first=False):
                act.wait_ge(x_in_slot[s], 16 * (turn + 1))
                if not first:
                    act.wait_ge(x_used, group - SLOTS + 1)
                nc.scalar.activation(x_hi[:, s, :], x_raw[:, s, :], ACT.Copy).then_inc(x_hi_ready, 1)

            def evacuate(q):
                for m in range(M_TILES):
                    if m < M_TILES - 1:
                        act.wait_ge(first_acc_ready, q + 1)
                    else:
                        act.wait_ge(x_used, GROUPS * (q + 1))
                    nc.scalar.activation(colours[:, m, :], acc[:, bass.ds(2 * q + m, 1), :]
                                         .rearrange("p a n -> p (a n)"), ACT.Identity,
                                         bias=params[:, B_IN_AT + m:B_IN_AT + m + 1]
                                         ).then_inc(colours_ready, 1)

            def relu1(q):
                act.wait_ge(layer1_ready, q + 1)
                nc.scalar.activation(h2[0:NARROW, :], layer1, ACT.Relu,
                                     bias=params[0:NARROW, B1_AT:B1_AT + 1]).then_inc(relu1_ready, 1)

            def write_scores(q):
                act.wait_ge(layer3_ready, q + 1)
                nc.scalar.activation(scores[0:1, bass.ds(q * Q_ROWS, Q_ROWS)], layer3[0:1, :],
                                     ACT.Copy).then_inc(scores_ready, 1)

            for s in range(SLOTS):
                split_w(0, s, s)
                split_x(0, s, s, first=True)
            with act.Fori(1, TURNS) as turn:
                for s in range(SLOTS):
                    split_w(turn, s, turn * SLOTS + s)
                    split_x(turn, s, turn * SLOTS + s)
            act.wait_ge(params_in, 16)
            with act.Fori(1, QUARTERS) as q:
                for t in range(TURNS):
                    for s in range(SLOTS):
                        split_x(q * TURNS + t, s, q * GROUPS + t * SLOTS + s)
                        if t * SLOTS + s == LAYER1_AFTER + SLOTS - 1:
                            relu1(q - 1)
                        if t * SLOTS + s == LAYER3_AFTER + SLOTS - 1:
                            write_scores(q - 1)
                    if t == 0:
                        evacuate(q - 1)
            evacuate(QUARTERS - 1)
            relu1(QUARTERS - 1)
            write_scores(QUARTERS - 1)

        @block.vector
        def _(dve):
            def split_w(group, s):
                dve.wait_ge(w_hi_ready, group + 1)
                cols = bass.ds(group * (GROUP * HIDDEN), GROUP * HIDDEN)
                nc.vector.tensor_tensor(w_lo[:, cols], w_raw[:, s, :], w_hi[:, cols].bitcast(f32),
                                        ALU.subtract).then_inc(w_lo_ready, 1)

            def split_x(group, s):
                dve.wait_ge(x_hi_ready, group + 1)
                nc.vector.tensor_tensor(x_lo[:, s, :], x_raw[:, s, :], x_hi[:, s, :].bitcast(f32),
                                        ALU.subtract).then_inc(x_lo_ready, 1)

            def mix(q):
                for m in range(M_TILES):
                    white = colours[:, m, 0:Q_ROWS]
                    black = colours[:, m, Q_ROWS:2 * Q_ROWS]
                    done = STEPS * (M_TILES * q + m)
                    dve.wait_ge(colours_ready, M_TILES * q + m + 1)
                    nc.vector.tensor_tensor(swing[:, m, :], white, black, ALU.subtract
                                            ).then_inc(swing_step, 1)
                    dve.wait_ge(swing_step, done + 1)
                    nc.vector.tensor_tensor(swing[:, m, :], swing[:, m, :],
                                            side[:, bass.ds(q * Q_ROWS, Q_ROWS)], ALU.mult
                                            ).then_inc(swing_step, 1)
                    dve.wait_ge(swing_step, done + 2)
                    nc.vector.tensor_tensor(h1[:, m, 0, :], black, swing[:, m, :], ALU.add
                                            ).then_inc(swing_step, 1)
                    nc.vector.tensor_tensor(h1[:, m, 1, :], white, swing[:, m, :], ALU.subtract
                                            ).then_inc(swing_step, 1)
                    dve.wait_ge(swing_step, done + 4)
                    nc.vector.tensor_scalar(h1[:, m, :, :], h1[:, m, :, :], 0.0, 1.0, ALU.max, ALU.min
                                            ).then_inc(h1_ready, 1)

            def cap2(q):
                dve.wait_ge(relu1_ready, q + 1)
                nc.vector.tensor_scalar(h2[0:NARROW, :], h2[0:NARROW, :], 1.0, None, ALU.min
                                        ).then_inc(h2_ready, 1)

            def clip3(q):
                dve.wait_ge(layer2_ready, q + 1)
                nc.vector.tensor_scalar(h3[0:NARROW, :], layer2[0:NARROW, :], 0.0, 1.0, ALU.max, ALU.min
                                        ).then_inc(h3_ready, 1)

            with dve.Fori(0, TURNS) as turn:
                for s in range(SLOTS):
                    split_w(turn * SLOTS + s, s)
                    split_x(turn * SLOTS + s, s)
            dve.wait_ge(side_in, 16)
            with dve.Fori(1, QUARTERS) as q:
                for t in range(TURNS):
                    for s in range(SLOTS):
                        split_x(q * GROUPS + t * SLOTS + s, s)
                        if t * SLOTS + s == LAYER1_AFTER + SLOTS - 1:
                            cap2(q - 1)
                        if t * SLOTS + s == LAYER2_AFTER + SLOTS - 1:
                            clip3(q - 1)
                    if t == 0:
                        mix(q - 1)
            mix(QUARTERS - 1)
            cap2(QUARTERS - 1)
            clip3(QUARTERS - 1)

        @block.tensor
        def _(pe):
            def multiply(q, g, first_quarter=False):
                s = g % SLOTS
                if first_quarter:
                    pe.wait_ge(w_hi_ready, g + 1)
                pe.wait_ge(x_hi_ready, q * GROUPS + g + 1)
                if first_quarter:
                    pe.wait_ge(w_lo_ready, g + 1)
                pe.wait_ge(x_lo_ready, q * GROUPS + g + 1)
                for m in range(M_TILES):
                    bank = acc[:, bass.ds(2 * q + m, 1), :].rearrange("p a n -> p (a n)")
                    for k in range(GROUP):
                        at = (g * GROUP + k) * HIDDEN + m * P
                        wh, wl = w_hi[:, at:at + P], w_lo[:, at:at + P]
                        xh, xl = (x[:, s, k * COLS:(k + 1) * COLS] for x in (x_hi, x_lo))
                        opens, closes = g == 0 and k == 0, g == GROUPS - 1 and k == GROUP - 1
                        nc.tensor.matmul(bank, wh, xh, start=opens, stop=False)
                        nc.tensor.matmul(bank, wh, xl, start=False, stop=False)
                        last = nc.tensor.matmul(bank, wl, xh, start=False, stop=closes)
                        if closes and m < M_TILES - 1:
                            last.then_inc(first_acc_ready, 1)
                last.then_inc(x_used, 1)

            def small_layer1(q):
                pe.wait_ge(h1_ready, M_TILES * (q + 1))
                for m in range(M_TILES):
                    for half in range(2):
                        c = half * M_TILES + m
                        last = nc.tensor.matmul(
                            layer1, params[:, W1_AT + c * NARROW:W1_AT + (c + 1) * NARROW],
                            h1[:, m, half, :], start=m == 0 and half == 0,
                            stop=m == M_TILES - 1 and half == 1)
                last.then_inc(layer1_ready, 1)

            def small_layer2(q):
                pe.wait_ge(h2_ready, q + 1)
                nc.tensor.matmul(layer2, params[0:NARROW + 1, W2_AT:W2_AT + P], h2[:, :],
                                 start=True, stop=True).then_inc(layer2_ready, 1)

            def small_layer3(q):
                pe.wait_ge(h3_ready, q + 1)
                nc.tensor.matmul(layer3, params[0:NARROW + 1, W3_AT:W3_AT + P], h3[:, :],
                                 start=True, stop=True).then_inc(layer3_ready, 1)

            for g in range(GROUPS):
                multiply(0, g, first_quarter=True)
            pe.wait_ge(params_in, 16)
            pe.wait_ge(ones_ready, 2)
            with pe.Fori(1, QUARTERS) as q:
                for g in range(GROUPS):
                    multiply(q, g)
                    if g == LAYER1_AFTER:
                        small_layer1(q - 1)
                    if g == LAYER2_AFTER:
                        small_layer2(q - 1)
                    if g == LAYER3_AFTER:
                        small_layer3(q - 1)
            small_layer1(QUARTERS - 1)
            small_layer2(QUARTERS - 1)
            small_layer3(QUARTERS - 1)


def _lay_out(r_w_features, r_b_features, r_white_to_move, W_in, b_in, W1, b1, W2, b2, W3, b3):
    def stream(x):
        return np.asarray(x).reshape(QUARTERS, Q_ROWS, GROUPS, GROUP, P).transpose(0, 2, 4, 3, 1)

    features = np.stack([stream(r_w_features), stream(r_b_features)], axis=4)
    features = np.ascontiguousarray(features).reshape(QUARTERS * GROUPS, P, GROUP * COLS)
    w_in = np.ascontiguousarray(np.asarray(W_in).reshape(HIDDEN, K_TILES, P).transpose(2, 1, 0))
    small = np.zeros((P, SMALL_COLS), np.float32)
    small[:, W1_AT:B_IN_AT] = np.asarray(W1).reshape(NARROW, MLP_CHUNKS, P).transpose(2, 1, 0).reshape(P, -1)
    small[:, B_IN_AT:B1_AT] = np.asarray(b_in).reshape(M_TILES, P).T
    small[:NARROW, B1_AT] = np.asarray(b1)
    small[:NARROW, W2_AT:W2_AT + NARROW] = np.asarray(W2).T
    small[NARROW, W2_AT:W2_AT + NARROW] = np.asarray(b2)
    small[:NARROW, W3_AT] = np.asarray(W3)[0]
    small[NARROW, W3_AT] = np.asarray(b3)[0]
    return {
        "features": features,
        "w_in": w_in.reshape(P, K_TILES * HIDDEN),
        "white_to_move": np.ascontiguousarray(r_white_to_move).reshape(1, ROWS),
        "small": small,
    }


def kernel(r_w_features, r_b_features, r_white_to_move, L0_rec_W_in, L0_rec_b_in, L0_rec_W1, L0_rec_b1,
           L0_rec_W2, L0_rec_b2, L0_rec_W3, L0_rec_b3):
    import concourse.bacc as bacc
    from concourse.bass_utils import run_bass_kernel_spmd

    arrays = _lay_out(r_w_features, r_b_features, r_white_to_move, L0_rec_W_in, L0_rec_b_in, L0_rec_W1,
                      L0_rec_b1, L0_rec_W2, L0_rec_b2, L0_rec_W3, L0_rec_b3)
    nc = bacc.Bacc("TRN2", target_bir_lowering=False, num_devices=1)
    args = [nc.dram_tensor(f"{n}_dram", a.shape, mybir.dt.float32, kind="ExternalInput").ap()
            for n, a in arrays.items()]
    out = nc.dram_tensor("scores_dram", (1, ROWS), mybir.dt.float32, kind="ExternalOutput").ap()
    nnue_program(nc, *args, out)
    result = run_bass_kernel_spmd(nc, [{f"{n}_dram": a for n, a in arrays.items()}], core_ids=[0])
    return result.results[0]["scores_dram"].reshape(ROWS, 1)
```

```python
import numpy as np
import concourse.bass as bass
import concourse.mybir as mybir
from concourse.alu_op_type import AluOpType as ALU

ROWS = 1024
FEATURES = 5120
HIDDEN = 256
NARROW = 32
P = 128
K_TILES = FEATURES // P
M_TILES = HIDDEN // P
QUARTERS = 4
Q_ROWS = ROWS // QUARTERS
COLS = 2 * Q_ROWS
GROUP = 2
GROUPS = K_TILES // GROUP
SLOTS = 4
TURNS = GROUPS // SLOTS
ALL_TURNS = TURNS * QUARTERS
MLP_CHUNKS = 2 * HIDDEN // P
LAYER1_AFTER, LAYER2_AFTER, LAYER3_AFTER = 7, 12, 15
MIX_AFTER, RECTIFY_AFTER = 3, 5

BLOCKS = P // NARROW
B_ROWS = Q_ROWS // BLOCKS
LATE = 3
HALVES = 2
H_ROWS = Q_ROWS // HALVES
PIECES = [(m, h) for h in range(HALVES) for m in range(M_TILES)]
WARM_UP = 11

W1_AT = 0
B_IN_AT = W1_AT + MLP_CHUNKS * NARROW
B1_AT = B_IN_AT + M_TILES
B2_AT = B1_AT + 1
B3_AT = B2_AT + 1
W2_AT = B3_AT + 1
W3_AT = W2_AT + P
B1_ROW_AT = W3_AT + BLOCKS
B2_ROW_AT = B1_ROW_AT + P
B3_ROW_AT = B2_ROW_AT + P
SMALL_COLS = B3_ROW_AT + BLOCKS


def nnue_program(nc, features, w_in, white_to_move, small, out):
    f32, f32r = mybir.dt.float32, mybir.dt.float32r
    ACT = mybir.ActivationFunctionType

    from contextlib import ExitStack
    with ExitStack() as ctx:
        def sb(name, shape, dt=f32):
            return ctx.enter_context(nc.sbuf_tensor(name, shape, dt))

        def sem(name):
            return ctx.enter_context(nc.semaphore(name))

        w_hi = sb("w_hi", [P, K_TILES * HIDDEN], f32r)
        w_lo = sb("w_lo", [P, K_TILES * HIDDEN], f32r)
        w_raw = sb("w_raw", [P, SLOTS, GROUP * HIDDEN])
        x_raw = sb("x_raw", [P, SLOTS, GROUP * COLS])
        x_hi = sb("x_hi", [P, SLOTS, GROUP * COLS], f32r)
        x_lo = sb("x_lo", [P, SLOTS, GROUP * COLS], f32r)
        params = sb("params", [P, SMALL_COLS])
        side = sb("side", [P, ROWS])
        colours = sb("colours", [P, M_TILES, 2, Q_ROWS])
        swing = sb("swing", [P, M_TILES, Q_ROWS])
        mixed = sb("mixed", [P, M_TILES, 2, Q_ROWS])
        rect = sb("rect", [P, M_TILES, 2, Q_ROWS])
        h1_hi = sb("h1_hi", [P, M_TILES, 2, Q_ROWS], f32r)
        h1_lo = sb("h1_lo", [P, M_TILES, 2, Q_ROWS], f32r)
        w1_parts = sb("w1_parts", [P, MLP_CHUNKS, P], f32r)
        low1 = sb("low1", [NARROW, Q_ROWS])
        pre2 = sb("pre2", [NARROW, Q_ROWS])
        h2 = sb("h2", [P, B_ROWS])
        rect3 = sb("rect3", [P, B_ROWS])
        h3 = sb("h3", [P, B_ROWS])
        ones = sb("ones", [1, B_ROWS])
        zeros = sb("zeros", [P, 512], mybir.dt.bfloat16)
        scores = sb("scores", [BLOCKS, QUARTERS * B_ROWS])
        acc = ctx.enter_context(nc.psum_tensor("acc", [P, 2 * QUARTERS, 512], f32))
        layer1 = acc[:, 0, 0:Q_ROWS]
        layer2 = acc[:, 0, Q_ROWS:Q_ROWS + B_ROWS]
        layer3 = acc[0:BLOCKS, 1, 0:B_ROWS]
        last1 = acc[:, 2, 0:B_ROWS]
        last2 = acc[:, 3, 0:B_ROWS]
        last3 = acc[0:BLOCKS, 4, 0:B_ROWS]
        warm_out = acc[:, 2 * QUARTERS - 1, :]

        params_in = sem("params_in")
        side_in = sem("side_in")
        w_in_slot = [sem(f"w_in_slot{s}") for s in range(SLOTS)]
        x_in_slot = [sem(f"x_in_slot{s}") for s in range(SLOTS)]
        w_in_slice = [[sem(f"w_in_slot{s}_slice{k}") for k in range(GROUP - 1)] + [w_in_slot[s]]
                      for s in range(SLOTS)]
        x_in_slice = [[sem(f"x_in_slot{s}_slice{k}") for k in range(GROUP - 1)] + [x_in_slot[s]]
                      for s in range(SLOTS)]
        first_w_hi_ready = sem("first_w_hi_ready")
        w_hi_ready = sem("w_hi_ready")
        w_lo_ready = sem("w_lo_ready")
        x_hi_ready = sem("x_hi_ready")
        x_lo_ready = sem("x_lo_ready")
        x_used = sem("x_used")
        zeros_ready = sem("zeros_ready")
        ones_ready = sem("ones_ready")
        colours_ready = sem("colours_ready")
        mix_step = sem("mix_step")
        rect_ready = sem("rect_ready")
        h1_hi_ready = sem("h1_hi_ready")
        h1_ready = sem("h1_ready")
        w1_zero = sem("w1_zero")
        w1_hi_ready = sem("w1_hi_ready")
        w1_ready = sem("w1_ready")
        layer1_ready = sem("layer1_ready")
        low1_ready = sem("low1_ready")
        pre2_ready = sem("pre2_ready")
        h2_ready = sem("h2_ready")
        layer2_ready = sem("layer2_ready")
        rect3_ready = sem("rect3_ready")
        h3_ready = sem("h3_ready")
        layer3_ready = sem("layer3_ready")
        scores_ready = sem("scores_ready")
        piece_acc_ready = sem("piece_acc_ready")
        piece_out = sem("piece_out")
        piece_step = sem("piece_step")
        last1_ready = sem("last1_ready")
        last_h2_ready = sem("last_h2_ready")
        last2_ready = sem("last2_ready")
        last_h3_ready = sem("last_h3_ready")
        last3_ready = sem("last3_ready")
        last_scores_ready = sem("last_scores_ready")
        PIECE_STEPS = 5
        out_done = sem("out_done")
        MIX_STEPS = 4
        mixed_steps = lambda q, m: MIX_STEPS * (M_TILES * q + m)

        def w_slice(k, m=0, width=HIDDEN):
            return bass.ds(k * HIDDEN + m * P, width)

        def x_slice(k):
            return slice(k * COLS, (k + 1) * COLS)

        TURN_SLICES = [(s, k) for s in range(SLOTS) for k in range(GROUP)]

        block = ctx.enter_context(nc.Block())

        @block.sync
        def _(sp):
            def load_slice(turn, s, k, weights=True):
                if weights:
                    sp.dma_start(w_raw[:, s, w_slice(k)], w_in[:, w_slice((turn * SLOTS + s) * GROUP + k)]
                                 ).then_inc(w_in_slice[s][k], 16)
                sp.dma_start(x_raw[:, s, x_slice(k)], features[bass.ds(turn * SLOTS + s, 1), :, x_slice(k)]
                             .rearrange("a p n -> (a p) n")).then_inc(x_in_slice[s][k], 16)

            def load_x(group, s):
                sp.dma_start(x_raw[:, s, :], features[bass.ds(group, 1), :, :].rearrange("a p n -> (a p) n")
                             ).then_inc(x_in_slot[s], 16)

            for s, k in TURN_SLICES:
                load_slice(0, s, k, weights=(s, k) != TURN_SLICES[0])
            with sp.Fori(1, TURNS) as turn:
                for s, k in TURN_SLICES:
                    sp.wait_ge(x_lo_ready, ((turn - 1) * SLOTS + s) * GROUP + k + 1)
                    load_slice(turn, s, k)
            with sp.Fori(TURNS, ALL_TURNS) as turn:
                for s in range(SLOTS):
                    sp.wait_ge(x_lo_ready, ((turn - 1) * SLOTS + s + 1) * GROUP)
                    load_x(turn * SLOTS + s, s)
            sp.wait_ge(scores_ready, QUARTERS - 1)
            sp.wait_ge(last_scores_ready, 1)
            sp.dma_start(out.rearrange("a (q b r) -> (a b) q r", q=QUARTERS, b=BLOCKS),
                         scores[:, :].rearrange("b (q r) -> b q r", q=QUARTERS)).then_inc(out_done, 16)
            sp.wait_ge(out_done, 16)

        @block.gpsimd
        def _(pool):
            pool.dma_start(params[:, :], small).then_inc(params_in, 16)
            pool.dma_start(side[:, :], white_to_move.to_broadcast([P, ROWS])).then_inc(side_in, 16)
            nc.gpsimd.memset(ones[:, :], 1.0).then_inc(ones_ready, 1)
            nc.gpsimd.memset(w1_parts[:, :, 2 * NARROW:].bitcast(f32), 0.0).then_inc(w1_zero, 1)

        @block.scalar
        def _(act):
            def split_slice(turn, s, k, weights=True):
                if weights:
                    act.wait_ge(w_in_slice[s][k], 16 * (turn + 1))
                    nc.scalar.activation(w_hi[:, w_slice((turn * SLOTS + s) * GROUP + k)],
                                         w_raw[:, s, w_slice(k)], ACT.Copy).then_inc(w_hi_ready, 1)
                act.wait_ge(x_in_slice[s][k], 16 * (turn + 1))
                nc.scalar.activation(x_hi[:, s, x_slice(k)], x_raw[:, s, x_slice(k)], ACT.Copy
                                     ).then_inc(x_hi_ready, 1)

            def split_x(turn, s, group):
                act.wait_ge(x_in_slot[s], 16 * (turn + 1))
                act.wait_ge(x_used, group - SLOTS + 1)
                nc.scalar.activation(x_hi[:, s, :], x_raw[:, s, :], ACT.Copy).then_inc(x_hi_ready, GROUP)

            def evacuate(q, m):
                act.wait_ge(x_used, GROUPS * (q + 1))
                nc.scalar.activation(colours[:, m, :, :], acc[:, bass.ds(2 * q + m, 1), :]
                                     .rearrange("p a (c n) -> p (a c) n", c=2), ACT.Identity,
                                     bias=params[:, B_IN_AT + m:B_IN_AT + m + 1]
                                     ).then_inc(colours_ready, 1)

            def rectify(q, m):
                act.wait_ge(mix_step, mixed_steps(q, m) + MIX_STEPS)
                nc.scalar.activation(rect[:, m, :, :], mixed[:, m, :, :], ACT.Relu
                                     ).then_inc(rect_ready, 1)

            def rectify3(q):
                act.wait_ge(layer2_ready, q + 1)
                nc.scalar.activation(rect3[:, :], layer2, ACT.Relu,
                                     bias=params[:, B2_AT:B2_AT + 1]).then_inc(rect3_ready, 1)

            def write_scores(q):
                act.wait_ge(layer3_ready, q + 1)
                nc.scalar.activation(scores[:, bass.ds(q * B_ROWS, B_ROWS)], layer3, ACT.Identity,
                                     bias=params[0:BLOCKS, B3_AT:B3_AT + 1]).then_inc(scores_ready, 1)

            act.dma_start(w_raw[:, 0, w_slice(0)], w_in[:, w_slice(0)]).then_inc(w_in_slice[0][0], 16)
            for s, k in TURN_SLICES:
                split_slice(0, s, k, weights=(s, k) != TURN_SLICES[0])
            with act.Fori(1, TURNS) as turn:
                for s, k in TURN_SLICES:
                    if k == 0:
                        act.wait_ge(x_used, (turn - 1) * SLOTS + s + 1)
                    split_slice(turn, s, k)
            act.wait_ge(params_in, 16)
            nc.scalar.activation(w1_parts[:, :, 0:NARROW], params[:, W1_AT:B_IN_AT].rearrange(
                "p (c n) -> p c n", c=MLP_CHUNKS), ACT.Copy).then_inc(w1_hi_ready, 1)
            with act.Fori(1, QUARTERS) as q:
                for g in range(GROUPS):
                    split_x(q * TURNS + g // SLOTS, g % SLOTS, q * GROUPS + g)
                    if g == MIX_AFTER:
                        for m in range(M_TILES):
                            evacuate(q - 1, m)
                    if g == RECTIFY_AFTER:
                        for m in range(M_TILES):
                            rectify(q - 1, m)
                    if g == LAYER2_AFTER + SLOTS - 1:
                        rectify3(q - 1)
                    if g == GROUPS - 1:
                        write_scores(q - 1)
            for n, (m, h) in enumerate(PIECES):
                rows = slice(h * H_ROWS, (h + 1) * H_ROWS)
                act.wait_ge(piece_acc_ready, n + 1)
                nc.scalar.activation(colours[:, m, :, rows],
                                     acc[:, 2 * (QUARTERS - 1) + m, :]
                                     .rearrange("p (c n) -> p c n", c=2)[:, :, rows], ACT.Identity,
                                     bias=params[:, B_IN_AT + m:B_IN_AT + m + 1]
                                     ).then_inc(piece_out, 1)

        @block.vector
        def _(dve):
            def split_slice(turn, s, k, first=False):
                at = (turn * SLOTS + s) * GROUP + k
                if first:
                    dve.wait_ge(first_w_hi_ready, 1)
                else:
                    dve.wait_ge(w_hi_ready, at)
                nc.vector.tensor_tensor(w_lo[:, w_slice(at)], w_raw[:, s, w_slice(k)],
                                        w_hi[:, w_slice(at)].bitcast(f32), ALU.subtract
                                        ).then_inc(w_lo_ready, 1)
                dve.wait_ge(x_hi_ready, at + 1)
                nc.vector.tensor_tensor(x_lo[:, s, x_slice(k)], x_raw[:, s, x_slice(k)],
                                        x_hi[:, s, x_slice(k)].bitcast(f32), ALU.subtract
                                        ).then_inc(x_lo_ready, 1)

            def split_x(group, s):
                dve.wait_ge(x_hi_ready, (group + 1) * GROUP)
                nc.vector.tensor_tensor(x_lo[:, s, :], x_raw[:, s, :], x_hi[:, s, :].bitcast(f32),
                                        ALU.subtract).then_inc(x_lo_ready, GROUP)

            def mix(q, m):
                white, black = colours[:, m, 0, :], colours[:, m, 1, :]
                done = mixed_steps(q, m)
                dve.wait_ge(colours_ready, M_TILES * q + m + 1)
                nc.vector.tensor_tensor(swing[:, m, :], white, black, ALU.subtract
                                        ).then_inc(mix_step, 1)
                dve.wait_ge(mix_step, done + 1)
                nc.vector.tensor_tensor(swing[:, m, :], swing[:, m, :],
                                        side[:, bass.ds(q * Q_ROWS, Q_ROWS)], ALU.mult
                                        ).then_inc(mix_step, 1)
                dve.wait_ge(mix_step, done + 2)
                nc.vector.tensor_tensor(mixed[:, m, 0, :], black, swing[:, m, :], ALU.add
                                        ).then_inc(mix_step, 1)
                nc.vector.tensor_tensor(mixed[:, m, 1, :], white, swing[:, m, :], ALU.subtract
                                        ).then_inc(mix_step, 1)

            def clip1(q, m):
                dve.wait_ge(mix_step, mixed_steps(q, m) + MIX_STEPS)
                nc.vector.tensor_scalar(h1_hi[:, m, :, :], mixed[:, m, :, :], 0.0, 1.0, ALU.max, ALU.min
                                        ).then_inc(h1_hi_ready, 1)
                dve.wait_ge(h1_hi_ready, M_TILES * q + m + 1)
                dve.wait_ge(rect_ready, M_TILES * q + m + 1)
                nc.vector.scalar_tensor_tensor(h1_lo[:, m, :, :], rect[:, m, :, :], 1.0,
                                               h1_hi[:, m, :, :].bitcast(f32), ALU.min, ALU.subtract
                                               ).then_inc(h1_ready, 1)

            def clip2(q):
                dve.wait_ge(layer1_ready, q + 1)
                nc.vector.tensor_copy(low1[:, :], layer1[NARROW:2 * NARROW, :]).then_inc(low1_ready, 1)
                dve.wait_ge(low1_ready, q + 1)
                nc.vector.scalar_tensor_tensor(pre2[:, :], layer1[0:NARROW, :],
                                               params[0:NARROW, B1_AT:B1_AT + 1], low1[:, :],
                                               ALU.add, ALU.add).then_inc(pre2_ready, 1)
                dve.wait_ge(pre2_ready, q + 1)
                for b in range(BLOCKS):
                    last = nc.vector.tensor_scalar(h2[b * NARROW:(b + 1) * NARROW, :],
                                                   pre2[:, b * B_ROWS:(b + 1) * B_ROWS],
                                                   0.0, 1.0, ALU.max, ALU.min)
                last.then_inc(h2_ready, 1)

            def cap3(q):
                dve.wait_ge(rect3_ready, q + 1)
                nc.vector.tensor_scalar(h3[:, :], rect3[:, :], 1.0, None, ALU.min).then_inc(h3_ready, 1)

            def mix_piece(n, m, h):
                rows = slice(h * H_ROWS, (h + 1) * H_ROWS)
                white, black = colours[:, m, 0, rows], colours[:, m, 1, rows]
                turn = swing[:, m, rows]
                done = PIECE_STEPS * n
                dve.wait_ge(piece_out, n + 1)
                nc.vector.tensor_tensor(turn, white, black, ALU.subtract).then_inc(piece_step, 1)
                dve.wait_ge(piece_step, done + 1)
                last_q = (QUARTERS - 1) * Q_ROWS
                nc.vector.tensor_tensor(turn, turn, side[:, last_q + h * H_ROWS:last_q + (h + 1) * H_ROWS],
                                        ALU.mult).then_inc(piece_step, 1)
                dve.wait_ge(piece_step, done + 2)
                nc.vector.tensor_tensor(mixed[:, m, 0, rows], black, turn, ALU.add).then_inc(piece_step, 1)
                nc.vector.tensor_tensor(mixed[:, m, 1, rows], white, turn, ALU.subtract
                                        ).then_inc(piece_step, 1)
                dve.wait_ge(piece_step, done + 4)
                nc.vector.tensor_scalar(mixed[:, m, :, rows], mixed[:, m, :, rows], 0.0, 1.0,
                                        ALU.max, ALU.min).then_inc(piece_step, 1)

            nc.vector.memset(zeros[:, :], 0.0).then_inc(zeros_ready, 1)
            dve.wait_ge(w_in_slice[0][0], 16)
            nc.vector.tensor_copy(w_hi[:, w_slice(0)], w_raw[:, 0, w_slice(0)]).then_inc(first_w_hi_ready, 1)
            for s, k in TURN_SLICES:
                split_slice(0, s, k, first=(s, k) == TURN_SLICES[0])
            with dve.Fori(1, TURNS) as turn:
                for s, k in TURN_SLICES:
                    split_slice(turn, s, k)
            dve.wait_ge(side_in, 16)
            dve.wait_ge(w1_hi_ready, 1)
            w1 = params[:, W1_AT:B_IN_AT].rearrange("p (c n) -> p c n", c=MLP_CHUNKS)
            nc.vector.tensor_tensor(w1_parts[:, :, NARROW:2 * NARROW], w1,
                                    w1_parts[:, :, 0:NARROW].bitcast(f32), ALU.subtract
                                    ).then_inc(w1_ready, 1)
            with dve.Fori(1, QUARTERS) as q:
                for g in range(GROUPS):
                    split_x(q * GROUPS + g, g % SLOTS)
                    if g == MIX_AFTER:
                        for m in range(M_TILES):
                            mix(q - 1, m)
                    if g == RECTIFY_AFTER:
                        for m in range(M_TILES):
                            clip1(q - 1, m)
                    if g == LAYER1_AFTER + SLOTS - 1:
                        clip2(q - 1)
                    if g == LAYER3_AFTER + SLOTS - 2:
                        cap3(q - 1)
            for n, (m, h) in enumerate(PIECES):
                mix_piece(n, m, h)
            dve.wait_ge(last1_ready, 1)
            nc.vector.tensor_scalar(h2[:, :], last1, 0.0, 1.0, ALU.max, ALU.min).then_inc(last_h2_ready, 1)
            dve.wait_ge(last2_ready, 1)
            nc.vector.tensor_scalar(h3[:, :], last2, 0.0, 1.0, ALU.max, ALU.min).then_inc(last_h3_ready, 1)
            dve.wait_ge(last3_ready, 1)
            nc.vector.tensor_copy(scores[:, (QUARTERS - 1) * B_ROWS:], last3).then_inc(last_scores_ready, 1)

        @block.tensor
        def _(pe):
            def bank(q, m):
                return acc[:, bass.ds(2 * q + m, 1), :].rearrange("p a n -> p (a n)")

            def parts(g, k, m):
                tile = w_slice(g * GROUP + k, m, P)
                return (w_hi[:, tile], w_lo[:, tile],
                        x_hi[:, g % SLOTS, x_slice(k)], x_lo[:, g % SLOTS, x_slice(k)])

            def multiply_first(g):
                for k in range(GROUP):
                    at = g * GROUP + k
                    tiles = [(bank(0, m), *parts(g, k, m)) for m in range(M_TILES)]
                    if at == 0:
                        pe.wait_ge(first_w_hi_ready, 1)
                    else:
                        pe.wait_ge(w_hi_ready, at)
                    pe.wait_ge(x_hi_ready, at + 1)
                    for to, wh, wl, xh, xl in tiles:
                        nc.tensor.matmul(to, wh, xh, start=at == 0, stop=False)
                    pe.wait_ge(w_lo_ready, at + 1)
                    for to, wh, wl, xh, xl in tiles:
                        nc.tensor.matmul(to, wl, xh, start=False, stop=False)
                    pe.wait_ge(x_lo_ready, at + 1)
                    for to, wh, wl, xh, xl in tiles:
                        last = nc.tensor.matmul(to, wh, xl, start=False,
                                                stop=at == (GROUPS - LATE) * GROUP - 1)
                last.then_inc(x_used, 1)

            def multiply(q, g, new_weights=False):
                if new_weights:
                    pe.wait_ge(w_hi_ready, (g + 1) * GROUP - 1)
                    pe.wait_ge(w_lo_ready, (g + 1) * GROUP)
                pe.wait_ge(x_hi_ready, (q * GROUPS + g + 1) * GROUP)
                pe.wait_ge(x_lo_ready, (q * GROUPS + g + 1) * GROUP)
                goes_on = g >= GROUPS - LATE
                for m in range(M_TILES):
                    for k in range(GROUP):
                        wh, wl, xh, xl = parts(g, k, m)
                        opens = g == 0 and k == 0
                        closes = g in (GROUPS - LATE - 1, GROUPS - 1) and k == GROUP - 1
                        nc.tensor.matmul(bank(q, m), wh, xh, start=opens, stop=False,
                                         skip_group_check=goes_on)
                        nc.tensor.matmul(bank(q, m), wh, xl, start=False, stop=False,
                                         skip_group_check=goes_on)
                        last = nc.tensor.matmul(bank(q, m), wl, xh, start=False, stop=closes,
                                                skip_group_check=goes_on)
                last.then_inc(x_used, 1)

            def multiply_piece(m, h):
                def split(x):
                    return x.rearrange("p (c n) -> p c n", c=2)[:, :, h * H_ROWS:(h + 1) * H_ROWS]

                first = (m, h) == PIECES[0]
                to = split(acc[:, 2 * (QUARTERS - 1) + m, :])
                for g in range(GROUPS - LATE, GROUPS):
                    if first:
                        ready = ((QUARTERS - 1) * GROUPS + g + 1) * GROUP
                        pe.wait_ge(x_hi_ready, ready)
                        pe.wait_ge(x_lo_ready, ready)
                    for k in range(GROUP):
                        wh, wl, xh, xl = parts(g, k, m)
                        closes = g == GROUPS - 1 and k == GROUP - 1
                        nc.tensor.matmul(to, wh, split(xh), start=False, stop=False, skip_group_check=True)
                        nc.tensor.matmul(to, wh, split(xl), start=False, stop=False, skip_group_check=True)
                        last = nc.tensor.matmul(to, wl, split(xh), start=False, stop=closes,
                                                skip_group_check=True)
                last.then_inc(piece_acc_ready, 1)

            def last_layer1(n, m, h):
                pe.wait_ge(piece_step, PIECE_STEPS * (n + 1))
                for half in range(2):
                    c = half * M_TILES + m
                    for b in range(h * BLOCKS // HALVES, (h + 1) * BLOCKS // HALVES):
                        last = nc.tensor.matmul(
                            last1[b * NARROW:(b + 1) * NARROW, :],
                            params[:, W1_AT + c * NARROW:W1_AT + (c + 1) * NARROW],
                            mixed[:, m, half, b * B_ROWS:(b + 1) * B_ROWS],
                            start=False, stop=m == M_TILES - 1 and half == 1, tile_position=(0, b * NARROW))
                if n == len(PIECES) - 1:
                    last.then_inc(last1_ready, 1)

            def small_layer1(q, m):
                pe.wait_ge(h1_ready, M_TILES * q + m + 1)
                for half in range(2):
                    for part in (h1_hi, h1_lo):
                        opens = m == 0 and half == 0 and part is h1_hi
                        closes = m == M_TILES - 1 and half == 1 and part is h1_lo
                        last = nc.tensor.matmul(layer1, w1_parts[:, half * M_TILES + m, :],
                                                part[:, m, half, :], start=opens, stop=closes)
                if m == M_TILES - 1:
                    last.then_inc(layer1_ready, 1)

            def small_layer2(q):
                pe.wait_ge(h2_ready, q + 1)
                nc.tensor.matmul(layer2, params[:, W2_AT:W2_AT + P], h2[:, :],
                                 start=True, stop=True).then_inc(layer2_ready, 1)

            def small_layer3(q):
                pe.wait_ge(h3_ready, q + 1)
                nc.tensor.matmul(layer3, params[:, W3_AT:W3_AT + BLOCKS], h3[:, :],
                                 start=True, stop=True).then_inc(layer3_ready, 1)

            pe.wait_ge(zeros_ready, 1)
            for _ in range(WARM_UP):
                nc.tensor.matmul(warm_out, zeros[:, 0:P], zeros[:, :], start=True, stop=True)
            for g in range(GROUPS - LATE):
                multiply_first(g)
            with pe.Fori(1, QUARTERS) as q:
                for g in range(GROUPS - LATE, GROUPS):
                    multiply(q - 1, g, new_weights=True)
                for g in range(GROUPS - LATE):
                    multiply(q, g)
                    if g == LAYER1_AFTER:
                        pe.wait_ge(w1_zero, 1)
                        pe.wait_ge(w1_ready, 1)
                        for m in range(M_TILES):
                            small_layer1(q - 1, m)
                    if g == LAYER2_AFTER:
                        small_layer2(q - 1)
                    if g == LAYER3_AFTER:
                        small_layer3(q - 1)
            pe.wait_ge(ones_ready, 1)
            for to, at, width in ((last1, B1_ROW_AT, P), (last2, B2_ROW_AT, P), (last3, B3_ROW_AT, BLOCKS)):
                nc.tensor.matmul(to, params[0:1, at:at + width], ones[:, :], start=True, stop=False)
            for n, (m, h) in enumerate(PIECES):
                if n >= M_TILES:
                    pe.wait_ge(piece_out, n - M_TILES + 1)
                multiply_piece(m, h)
                if n >= 1:
                    last_layer1(n - 1, *PIECES[n - 1])
            last_layer1(len(PIECES) - 1, *PIECES[-1])
            pe.wait_ge(last_h2_ready, 1)
            nc.tensor.matmul(last2, params[:, W2_AT:W2_AT + P], h2[:, :],
                             start=False, stop=True).then_inc(last2_ready, 1)
            pe.wait_ge(last_h3_ready, 1)
            nc.tensor.matmul(last3, params[:, W3_AT:W3_AT + BLOCKS], h3[:, :],
                             start=False, stop=True).then_inc(last3_ready, 1)


def _lay_out(r_w_features, r_b_features, r_white_to_move, W_in, b_in, W1, b1, W2, b2, W3, b3):
    def stream(x):
        return np.asarray(x).reshape(QUARTERS, Q_ROWS, GROUPS, GROUP, P).transpose(0, 2, 4, 3, 1)

    features = np.stack([stream(r_w_features), stream(r_b_features)], axis=4)
    features = np.ascontiguousarray(features).reshape(QUARTERS * GROUPS, P, GROUP * COLS)
    w_in = np.ascontiguousarray(np.asarray(W_in).reshape(HIDDEN, K_TILES, P).transpose(2, 1, 0))
    small = np.zeros((P, SMALL_COLS), np.float32)
    small[:, W1_AT:B_IN_AT] = np.asarray(W1).reshape(NARROW, MLP_CHUNKS, P).transpose(2, 1, 0).reshape(P, -1)
    small[:, B_IN_AT:B1_AT] = np.asarray(b_in).reshape(M_TILES, P).T
    small[:NARROW, B1_AT] = np.asarray(b1)
    small[0, B1_ROW_AT:B2_ROW_AT] = np.tile(np.asarray(b1), BLOCKS)
    small[0, B2_ROW_AT:B3_ROW_AT] = np.tile(np.asarray(b2), BLOCKS)
    small[0, B3_ROW_AT:SMALL_COLS] = np.asarray(b3)[0]
    for b in range(BLOCKS):
        rows = slice(b * NARROW, (b + 1) * NARROW)
        small[rows, B2_AT] = np.asarray(b2)
        small[b, B3_AT] = np.asarray(b3)[0]
        small[rows, W2_AT + b * NARROW:W2_AT + (b + 1) * NARROW] = np.asarray(W2).T
        small[rows, W3_AT + b] = np.asarray(W3)[0]
    return {
        "features": features,
        "w_in": w_in.reshape(P, K_TILES * HIDDEN),
        "white_to_move": np.ascontiguousarray(r_white_to_move).reshape(1, ROWS),
        "small": small,
    }


def kernel(r_w_features, r_b_features, r_white_to_move, L0_rec_W_in, L0_rec_b_in, L0_rec_W1, L0_rec_b1,
           L0_rec_W2, L0_rec_b2, L0_rec_W3, L0_rec_b3):
    import concourse.bacc as bacc
    from concourse.bass_utils import run_bass_kernel_spmd

    arrays = _lay_out(r_w_features, r_b_features, r_white_to_move, L0_rec_W_in, L0_rec_b_in, L0_rec_W1,
                      L0_rec_b1, L0_rec_W2, L0_rec_b2, L0_rec_W3, L0_rec_b3)
    nc = bacc.Bacc("TRN2", target_bir_lowering=False, num_devices=1)
    args = [nc.dram_tensor(f"{n}_dram", a.shape, mybir.dt.float32, kind="ExternalInput").ap()
            for n, a in arrays.items()]
    out = nc.dram_tensor("scores_dram", (1, ROWS), mybir.dt.float32, kind="ExternalOutput").ap()
    nnue_program(nc, *args, out)
    result = run_bass_kernel_spmd(nc, [{f"{n}_dram": a for n, a in arrays.items()}], core_ids=[0])
    return result.results[0]["scores_dram"].reshape(ROWS, 1)
```

```python
import numpy as np
import concourse.bass as bass
import concourse.mybir as mybir
from concourse.alu_op_type import AluOpType as ALU

ROWS = 1024
FEATURES = 5120
HIDDEN = 256
NARROW = 32
P = 128
K_TILES = FEATURES // P
M_TILES = HIDDEN // P
QUARTERS = 4
Q_ROWS = ROWS // QUARTERS
COLS = 2 * Q_ROWS
GROUP = 2
GROUPS = K_TILES // GROUP
SLOTS = 4
TURNS = GROUPS // SLOTS
ALL_TURNS = TURNS * QUARTERS
MLP_CHUNKS = 2 * HIDDEN // P
LAYER1_AFTER, LAYER2_AFTER, LAYER3_AFTER = 7, 12, 15
MIX_AFTER, CLIP1_AFTER = 3, 5
CLIP2_AFTER = LAYER1_AFTER + SLOTS - 1
RECTIFY3_AFTER, CAP3_AFTER = LAYER2_AFTER + SLOTS - 1, LAYER2_AFTER + SLOTS + 1
SCORES_AFTER = GROUPS - 1

BLOCKS = P // NARROW
B_ROWS = Q_ROWS // BLOCKS
LATE = 3
HALVES = 2
H_ROWS = Q_ROWS // HALVES
PIECES = [(m, h) for h in range(HALVES) for m in range(M_TILES)]
WARM_UP = 8

W1_AT = 0
B_IN_AT = W1_AT + MLP_CHUNKS * NARROW
B1_AT = B_IN_AT + M_TILES
B2_AT = B1_AT + 1
B3_AT = B2_AT + 1
W2_AT = B3_AT + 1
W3_AT = W2_AT + P
B1_ROW_AT = W3_AT + BLOCKS
B2_ROW_AT = B1_ROW_AT + P
B3_ROW_AT = B2_ROW_AT + P
SMALL_COLS = B3_ROW_AT + BLOCKS


def nnue_program(nc, features, w_in, white_to_move, small, out):
    f32, f32r = mybir.dt.float32, mybir.dt.float32r
    ACT = mybir.ActivationFunctionType

    from contextlib import ExitStack
    with ExitStack() as ctx:
        def sb(name, shape, dt=f32):
            return ctx.enter_context(nc.sbuf_tensor(name, shape, dt))

        def sem(name):
            return ctx.enter_context(nc.semaphore(name))

        w_hi = sb("w_hi", [P, K_TILES * HIDDEN], f32r)
        w_lo = sb("w_lo", [P, K_TILES * HIDDEN], f32r)
        w_raw = sb("w_raw", [P, SLOTS, GROUP * HIDDEN])
        x_raw = sb("x_raw", [P, SLOTS, GROUP * COLS])
        x_hi = sb("x_hi", [P, SLOTS, GROUP * COLS], f32r)
        x_lo = sb("x_lo", [P, SLOTS, GROUP * COLS], f32r)
        params = sb("params", [P, SMALL_COLS])
        weights = sb("weights", [P, 3, ROWS])
        terms = sb("terms", [P, M_TILES, 2, 2, Q_ROWS])
        mixed = sb("mixed", [P, M_TILES, 2, Q_ROWS])
        rect = sb("rect", [P, M_TILES, 2, Q_ROWS])
        h1_hi = sb("h1_hi", [P, M_TILES, 2, Q_ROWS], f32r)
        h1_lo = sb("h1_lo", [P, M_TILES, 2, Q_ROWS], f32r)
        w1_parts = sb("w1_parts", [P, MLP_CHUNKS, P], f32r)
        low1 = sb("low1", [NARROW, Q_ROWS])
        pre2 = sb("pre2", [NARROW, Q_ROWS])
        h2 = sb("h2", [P, B_ROWS])
        rect3 = sb("rect3", [P, B_ROWS])
        h3 = sb("h3", [P, B_ROWS])
        ones = sb("ones", [1, B_ROWS])
        zeros = sb("zeros", [P, 512], mybir.dt.bfloat16)
        scores = sb("scores", [BLOCKS, QUARTERS * B_ROWS])
        acc = ctx.enter_context(nc.psum_tensor("acc", [P, 2 * QUARTERS, 512], f32))
        layer1 = acc[:, 0, 0:Q_ROWS]
        layer2 = acc[:, 0, Q_ROWS:Q_ROWS + B_ROWS]
        layer3 = acc[0:BLOCKS, 1, 0:B_ROWS]
        last1 = acc[:, 2, 0:B_ROWS]
        last2 = acc[:, 3, 0:B_ROWS]
        last3 = acc[0:BLOCKS, 4, 0:B_ROWS]
        warm_out = acc[:, 2 * QUARTERS - 1, :]

        params_in = sem("params_in")
        side_in = sem("side_in")
        w_in_slot = [sem(f"w_in_slot{s}") for s in range(SLOTS)]
        x_in_slot = [sem(f"x_in_slot{s}") for s in range(SLOTS)]
        w_in_slice = [[sem(f"w_in_slot{s}_slice{k}") for k in range(GROUP - 1)] + [w_in_slot[s]]
                      for s in range(SLOTS)]
        x_in_slice = [[sem(f"x_in_slot{s}_slice{k}") for k in range(GROUP - 1)] + [x_in_slot[s]]
                      for s in range(SLOTS)]
        first_w_hi_ready = sem("first_w_hi_ready")
        w_hi_ready = sem("w_hi_ready")
        w_lo_ready = sem("w_lo_ready")
        x_hi_ready = sem("x_hi_ready")
        x_lo_ready = sem("x_lo_ready")
        x_used = sem("x_used")
        zeros_ready = sem("zeros_ready")
        ones_ready = sem("ones_ready")
        side_copied = sem("side_copied")
        side_ready = sem("side_ready")
        w1_zero = sem("w1_zero")
        w1_hi_ready = sem("w1_hi_ready")
        w1_ready = sem("w1_ready")
        mix_step = sem("mix_step")
        rect_ready = sem("rect_ready")
        h1_hi_ready = sem("h1_hi_ready")
        h1_ready = sem("h1_ready")
        layer1_ready = sem("layer1_ready")
        low1_ready = sem("low1_ready")
        pre2_ready = sem("pre2_ready")
        h2_ready = sem("h2_ready")
        layer2_ready = sem("layer2_ready")
        rect3_ready = sem("rect3_ready")
        h3_ready = sem("h3_ready")
        layer3_ready = sem("layer3_ready")
        scores_ready = sem("scores_ready")
        piece_acc_ready = sem("piece_acc_ready")
        piece_step = sem("piece_step")
        last1_ready = sem("last1_ready")
        last_h2_ready = sem("last_h2_ready")
        last2_ready = sem("last2_ready")
        last_h3_ready = sem("last_h3_ready")
        last3_ready = sem("last3_ready")
        last_scores_ready = sem("last_scores_ready")
        PIECE_STEPS = 4
        out_done = sem("out_done")
        MIX_STEPS = 3

        def mixed_steps(q, m):
            return MIX_STEPS * (M_TILES * q + m)

        def colours_of(columns):
            return columns.rearrange("p (c n) -> p c n", c=2)

        def half_rows(h):
            return slice(h * H_ROWS, (h + 1) * H_ROWS)

        def w_slice(k, m=0, width=HIDDEN):
            return bass.ds(k * HIDDEN + m * P, width)

        def x_slice(k):
            return slice(k * COLS, (k + 1) * COLS)

        SLICES_PER_TURN = SLOTS * GROUP
        TURN_SLICES = [(s, k) for s in range(SLOTS) for k in range(GROUP)]

        block = ctx.enter_context(nc.Block())

        @block.sync
        def _(sp):
            def load_slice(turn, s, k):
                sp.dma_start(w_raw[:, s, w_slice(k)], w_in[:, w_slice((turn * SLOTS + s) * GROUP + k)]
                             ).then_inc(w_in_slice[s][k], 16)
                sp.dma_start(x_raw[:, s, x_slice(k)], features[bass.ds(turn * SLOTS + s, 1), :, x_slice(k)]
                             .rearrange("a p n -> (a p) n")).then_inc(x_in_slice[s][k], 16)

            def load_x(group, s):
                sp.dma_start(x_raw[:, s, :], features[bass.ds(group, 1), :, :].rearrange("a p n -> (a p) n")
                             ).then_inc(x_in_slot[s], 16)

            for s, k in TURN_SLICES:
                load_slice(0, s, k)
            with sp.Fori(1, TURNS) as turn:
                for s, k in TURN_SLICES:
                    sp.wait_ge(x_lo_ready, ((turn - 1) * SLOTS + s) * GROUP + k + 1)
                    load_slice(turn, s, k)
            with sp.Fori(TURNS, ALL_TURNS) as turn:
                for s in range(SLOTS):
                    sp.wait_ge(x_lo_ready, ((turn - 1) * SLOTS + s + 1) * GROUP)
                    load_x(turn * SLOTS + s, s)
            sp.wait_ge(scores_ready, QUARTERS - 1)
            sp.wait_ge(last_scores_ready, 1)
            sp.dma_start(out.rearrange("a (q b r) -> (a b) q r", q=QUARTERS, b=BLOCKS),
                         scores[:, :].rearrange("b (q r) -> b q r", q=QUARTERS)).then_inc(out_done, 16)
            sp.wait_ge(out_done, 16)

        @block.gpsimd
        def _(pool):
            nc.gpsimd.memset(ones[:, :], 1.0).then_inc(ones_ready, 1)
            nc.gpsimd.memset(w1_parts[:, :, 2 * NARROW:].bitcast(f32), 0.0).then_inc(w1_zero, 1)
            pool.wait_ge(w_lo_ready, K_TILES - SLICES_PER_TURN)
            pool.dma_start(params[:, :], small).then_inc(params_in, 16)
            pool.dma_start(weights[:, 0, :], white_to_move.to_broadcast([P, ROWS])).then_inc(side_in, 16)

        @block.scalar
        def _(act):
            def split_slice(turn, s, k, weights=True):
                if weights:
                    act.wait_ge(w_in_slice[s][k], 16 * (turn + 1))
                    nc.scalar.activation(w_hi[:, w_slice((turn * SLOTS + s) * GROUP + k)],
                                         w_raw[:, s, w_slice(k)], ACT.Copy).then_inc(w_hi_ready, 1)
                act.wait_ge(x_in_slice[s][k], 16 * (turn + 1))
                nc.scalar.activation(x_hi[:, s, x_slice(k)], x_raw[:, s, x_slice(k)], ACT.Copy
                                     ).then_inc(x_hi_ready, 1)

            def split_x(turn, s, group):
                act.wait_ge(x_in_slot[s], 16 * (turn + 1))
                act.wait_ge(x_used, group - SLOTS + 1)
                nc.scalar.activation(x_hi[:, s, :], x_raw[:, s, :], ACT.Copy).then_inc(x_hi_ready, GROUP)

            def rectify(q, m):
                act.wait_ge(mix_step, mixed_steps(q, m) + MIX_STEPS)
                nc.scalar.activation(rect[:, m, :, :], mixed[:, m, :, :], ACT.Relu
                                     ).then_inc(rect_ready, 1)

            def rectify3(q):
                act.wait_ge(layer2_ready, q + 1)
                nc.scalar.activation(rect3[:, :], layer2, ACT.Relu,
                                     bias=params[:, B2_AT:B2_AT + 1]).then_inc(rect3_ready, 1)

            def write_scores(q):
                act.wait_ge(layer3_ready, q + 1)
                nc.scalar.activation(scores[:, bass.ds(q * B_ROWS, B_ROWS)], layer3, ACT.Identity,
                                     bias=params[0:BLOCKS, B3_AT:B3_AT + 1]).then_inc(scores_ready, 1)

            for s, k in TURN_SLICES:
                split_slice(0, s, k, weights=(s, k) != TURN_SLICES[0])
            with act.Fori(1, TURNS) as turn:
                for s, k in TURN_SLICES:
                    if k == 0:
                        act.wait_ge(x_used, (turn - 1) * SLOTS + s + 1)
                    split_slice(turn, s, k)
            act.wait_ge(params_in, 16)
            nc.scalar.activation(w1_parts[:, :, 0:NARROW], params[:, W1_AT:B_IN_AT].rearrange(
                "p (c n) -> p c n", c=MLP_CHUNKS), ACT.Copy).then_inc(w1_hi_ready, 1)
            act.wait_ge(side_in, 16)
            nc.scalar.activation(weights[:, 2, :], weights[:, 0, :], ACT.Copy).then_inc(side_copied, 1)
            with act.Fori(1, QUARTERS) as q:
                for g in range(GROUPS):
                    split_x(q * TURNS + g // SLOTS, g % SLOTS, q * GROUPS + g)
                    if g == CLIP1_AFTER:
                        for m in range(M_TILES):
                            rectify(q - 1, m)
                    if g == RECTIFY3_AFTER:
                        rectify3(q - 1)
                    if g == SCORES_AFTER:
                        write_scores(q - 1)

        @block.vector
        def _(dve):
            def split_slice(turn, s, k, first=False):
                at = (turn * SLOTS + s) * GROUP + k
                if first:
                    dve.wait_ge(first_w_hi_ready, 1)
                else:
                    dve.wait_ge(w_hi_ready, at)
                nc.vector.tensor_tensor(w_lo[:, w_slice(at)], w_raw[:, s, w_slice(k)],
                                        w_hi[:, w_slice(at)].bitcast(f32), ALU.subtract
                                        ).then_inc(w_lo_ready, 1)
                dve.wait_ge(x_hi_ready, at + 1)
                nc.vector.tensor_tensor(x_lo[:, s, x_slice(k)], x_raw[:, s, x_slice(k)],
                                        x_hi[:, s, x_slice(k)].bitcast(f32), ALU.subtract
                                        ).then_inc(x_lo_ready, 1)

            def split_x(group, s):
                dve.wait_ge(x_hi_ready, (group + 1) * GROUP)
                nc.vector.tensor_tensor(x_lo[:, s, :], x_raw[:, s, :], x_hi[:, s, :].bitcast(f32),
                                        ALU.subtract).then_inc(x_lo_ready, GROUP)

            def weigh(m, from_acc, rows, start, width, step):
                for half in range(2):
                    nc.vector.scalar_tensor_tensor(
                        terms[:, m, half, :, rows], from_acc, params[:, B_IN_AT + m:B_IN_AT + m + 1],
                        weights[:, half:half + 2, bass.ds(start, width)], ALU.add, ALU.mult
                        ).then_inc(step, 1)

            def mix(q, m):
                whole = slice(0, Q_ROWS)
                dve.wait_ge(x_used, GROUPS * (q + 1))
                weigh(m, colours_of(acc[:, bass.ds(2 * q + m, 1), :].rearrange("p a n -> p (a n)")), whole,
                      q * Q_ROWS, Q_ROWS, mix_step)
                dve.wait_ge(mix_step, mixed_steps(q, m) + 2)
                nc.vector.tensor_tensor(mixed[:, m, :, :], terms[:, m, :, 0, :], terms[:, m, :, 1, :],
                                        ALU.add).then_inc(mix_step, 1)

            def clip1(q, m):
                dve.wait_ge(mix_step, mixed_steps(q, m) + MIX_STEPS)
                nc.vector.tensor_scalar(h1_hi[:, m, :, :], mixed[:, m, :, :], 0.0, 1.0, ALU.max, ALU.min
                                        ).then_inc(h1_hi_ready, 1)
                dve.wait_ge(h1_hi_ready, M_TILES * q + m + 1)
                dve.wait_ge(rect_ready, M_TILES * q + m + 1)
                nc.vector.scalar_tensor_tensor(h1_lo[:, m, :, :], rect[:, m, :, :], 1.0,
                                               h1_hi[:, m, :, :].bitcast(f32), ALU.min, ALU.subtract
                                               ).then_inc(h1_ready, 1)

            def clip2(q):
                dve.wait_ge(layer1_ready, q + 1)
                nc.vector.tensor_copy(low1[:, :], layer1[NARROW:2 * NARROW, :]).then_inc(low1_ready, 1)
                dve.wait_ge(low1_ready, q + 1)
                nc.vector.scalar_tensor_tensor(pre2[:, :], layer1[0:NARROW, :],
                                               params[0:NARROW, B1_AT:B1_AT + 1], low1[:, :],
                                               ALU.add, ALU.add).then_inc(pre2_ready, 1)
                dve.wait_ge(pre2_ready, q + 1)
                for b in range(BLOCKS):
                    last = nc.vector.tensor_scalar(h2[b * NARROW:(b + 1) * NARROW, :],
                                                   pre2[:, b * B_ROWS:(b + 1) * B_ROWS],
                                                   0.0, 1.0, ALU.max, ALU.min)
                last.then_inc(h2_ready, 1)

            def cap3(q):
                dve.wait_ge(rect3_ready, q + 1)
                nc.vector.tensor_scalar(h3[:, :], rect3[:, :], 1.0, None, ALU.min).then_inc(h3_ready, 1)

            def mix_piece(n, m, h):
                rows = half_rows(h)
                done = PIECE_STEPS * n
                dve.wait_ge(piece_acc_ready, n + 1)
                weigh(m, colours_of(acc[:, 2 * (QUARTERS - 1) + m, :])[:, :, rows], rows,
                      (QUARTERS - 1) * Q_ROWS + h * H_ROWS, H_ROWS, piece_step)
                dve.wait_ge(piece_step, done + 2)
                nc.vector.tensor_tensor(mixed[:, m, :, rows], terms[:, m, :, 0, rows], terms[:, m, :, 1, rows],
                                        ALU.add).then_inc(piece_step, 1)
                dve.wait_ge(piece_step, done + 3)
                nc.vector.tensor_scalar(mixed[:, m, :, rows], mixed[:, m, :, rows], 0.0, 1.0,
                                        ALU.max, ALU.min).then_inc(piece_step, 1)

            nc.vector.memset(zeros[:, :], 0.0).then_inc(zeros_ready, 1)
            dve.wait_ge(w_in_slice[0][0], 16)
            nc.vector.tensor_copy(w_hi[:, w_slice(0)], w_raw[:, 0, w_slice(0)]).then_inc(first_w_hi_ready, 1)
            for s, k in TURN_SLICES:
                split_slice(0, s, k, first=(s, k) == TURN_SLICES[0])
            with dve.Fori(1, TURNS) as turn:
                for s, k in TURN_SLICES:
                    split_slice(turn, s, k)
            dve.wait_ge(side_in, 16)
            nc.vector.tensor_scalar(weights[:, 1, :], weights[:, 0, :], -1.0, 1.0, ALU.mult, ALU.add
                                    ).then_inc(side_ready, 1)
            dve.wait_ge(side_ready, 1)
            dve.wait_ge(side_copied, 1)
            dve.wait_ge(w1_hi_ready, 1)
            w1 = params[:, W1_AT:B_IN_AT].rearrange("p (c n) -> p c n", c=MLP_CHUNKS)
            nc.vector.tensor_tensor(w1_parts[:, :, NARROW:2 * NARROW], w1,
                                    w1_parts[:, :, 0:NARROW].bitcast(f32), ALU.subtract
                                    ).then_inc(w1_ready, 1)
            with dve.Fori(1, QUARTERS) as q:
                for g in range(GROUPS):
                    split_x(q * GROUPS + g, g % SLOTS)
                    if g == MIX_AFTER:
                        for m in range(M_TILES):
                            mix(q - 1, m)
                    if g == CLIP1_AFTER:
                        for m in range(M_TILES):
                            clip1(q - 1, m)
                    if g == CLIP2_AFTER:
                        clip2(q - 1)
                    if g == CAP3_AFTER:
                        cap3(q - 1)
            for n, (m, h) in enumerate(PIECES):
                mix_piece(n, m, h)
            dve.wait_ge(last1_ready, 1)
            nc.vector.tensor_scalar(h2[:, :], last1, 0.0, 1.0, ALU.max, ALU.min).then_inc(last_h2_ready, 1)
            dve.wait_ge(last2_ready, 1)
            nc.vector.tensor_scalar(h3[:, :], last2, 0.0, 1.0, ALU.max, ALU.min).then_inc(last_h3_ready, 1)
            dve.wait_ge(last3_ready, 1)
            nc.vector.tensor_copy(scores[:, (QUARTERS - 1) * B_ROWS:], last3).then_inc(last_scores_ready, 1)

        @block.tensor
        def _(pe):
            def bank(q, m):
                return acc[:, bass.ds(2 * q + m, 1), :].rearrange("p a n -> p (a n)")

            def parts(g, k, m):
                tile = w_slice(g * GROUP + k, m, P)
                return (w_hi[:, tile], w_lo[:, tile],
                        x_hi[:, g % SLOTS, x_slice(k)], x_lo[:, g % SLOTS, x_slice(k)])

            def multiply_first(g):
                for k in range(GROUP):
                    at = g * GROUP + k
                    tiles = [(bank(0, m), *parts(g, k, m)) for m in range(M_TILES)]
                    if at == 0:
                        pe.wait_ge(first_w_hi_ready, 1)
                    else:
                        pe.wait_ge(w_hi_ready, at)
                    pe.wait_ge(x_hi_ready, at + 1)
                    for to, wh, wl, xh, xl in tiles:
                        nc.tensor.matmul(to, wh, xh, start=at == 0, stop=False)
                    pe.wait_ge(w_lo_ready, at + 1)
                    for to, wh, wl, xh, xl in tiles:
                        nc.tensor.matmul(to, wl, xh, start=False, stop=False)
                    pe.wait_ge(x_lo_ready, at + 1)
                    for to, wh, wl, xh, xl in tiles:
                        last = nc.tensor.matmul(to, wh, xl, start=False,
                                                stop=at == (GROUPS - LATE) * GROUP - 1)
                last.then_inc(x_used, 1)

            def multiply(q, g, new_weights=False):
                if new_weights:
                    pe.wait_ge(w_hi_ready, (g + 1) * GROUP - 1)
                    pe.wait_ge(w_lo_ready, (g + 1) * GROUP)
                pe.wait_ge(x_hi_ready, (q * GROUPS + g + 1) * GROUP)
                pe.wait_ge(x_lo_ready, (q * GROUPS + g + 1) * GROUP)
                goes_on = g >= GROUPS - LATE
                for m in range(M_TILES):
                    for k in range(GROUP):
                        wh, wl, xh, xl = parts(g, k, m)
                        opens = g == 0 and k == 0
                        closes = g in (GROUPS - LATE - 1, GROUPS - 1) and k == GROUP - 1
                        nc.tensor.matmul(bank(q, m), wh, xh, start=opens, stop=False,
                                         skip_group_check=goes_on)
                        nc.tensor.matmul(bank(q, m), wh, xl, start=False, stop=False,
                                         skip_group_check=goes_on)
                        last = nc.tensor.matmul(bank(q, m), wl, xh, start=False, stop=closes,
                                                skip_group_check=goes_on)
                last.then_inc(x_used, 1)

            def multiply_piece(m, h):
                first = (m, h) == PIECES[0]
                to = colours_of(acc[:, 2 * (QUARTERS - 1) + m, :])[:, :, half_rows(h)]
                for g in range(GROUPS - LATE, GROUPS):
                    if first:
                        ready = ((QUARTERS - 1) * GROUPS + g + 1) * GROUP
                        pe.wait_ge(x_hi_ready, ready)
                        pe.wait_ge(x_lo_ready, ready)
                    for k in range(GROUP):
                        wh, wl, xh, xl = parts(g, k, m)
                        xh, xl = (colours_of(x)[:, :, half_rows(h)] for x in (xh, xl))
                        closes = g == GROUPS - 1 and k == GROUP - 1
                        nc.tensor.matmul(to, wh, xh, start=False, stop=False, skip_group_check=True)
                        nc.tensor.matmul(to, wh, xl, start=False, stop=False, skip_group_check=True)
                        last = nc.tensor.matmul(to, wl, xh, start=False, stop=closes,
                                                skip_group_check=True)
                last.then_inc(piece_acc_ready, 1)

            def last_layer1(n, m, h):
                pe.wait_ge(piece_step, PIECE_STEPS * (n + 1))
                for half in range(2):
                    c = half * M_TILES + m
                    for b in range(h * BLOCKS // HALVES, (h + 1) * BLOCKS // HALVES):
                        last = nc.tensor.matmul(
                            last1[b * NARROW:(b + 1) * NARROW, :],
                            params[:, W1_AT + c * NARROW:W1_AT + (c + 1) * NARROW],
                            mixed[:, m, half, b * B_ROWS:(b + 1) * B_ROWS],
                            start=False, stop=m == M_TILES - 1 and half == 1, tile_position=(0, b * NARROW))
                if n == len(PIECES) - 1:
                    last.then_inc(last1_ready, 1)

            def small_layer1(q, m):
                pe.wait_ge(h1_ready, M_TILES * q + m + 1)
                for half in range(2):
                    for part in (h1_hi, h1_lo):
                        opens = m == 0 and half == 0 and part is h1_hi
                        closes = m == M_TILES - 1 and half == 1 and part is h1_lo
                        last = nc.tensor.matmul(layer1, w1_parts[:, half * M_TILES + m, :],
                                                part[:, m, half, :], start=opens, stop=closes)
                if m == M_TILES - 1:
                    last.then_inc(layer1_ready, 1)

            def small_layer2(q):
                pe.wait_ge(h2_ready, q + 1)
                nc.tensor.matmul(layer2, params[:, W2_AT:W2_AT + P], h2[:, :],
                                 start=True, stop=True).then_inc(layer2_ready, 1)

            def small_layer3(q):
                pe.wait_ge(h3_ready, q + 1)
                nc.tensor.matmul(layer3, params[:, W3_AT:W3_AT + BLOCKS], h3[:, :],
                                 start=True, stop=True).then_inc(layer3_ready, 1)

            pe.wait_ge(zeros_ready, 1)
            for _ in range(WARM_UP):
                nc.tensor.matmul(warm_out, zeros[:, 0:P], zeros[:, :], start=True, stop=True)
            for g in range(GROUPS - LATE):
                multiply_first(g)
            with pe.Fori(1, QUARTERS) as q:
                for g in range(GROUPS - LATE, GROUPS):
                    multiply(q - 1, g, new_weights=True)
                for g in range(GROUPS - LATE):
                    multiply(q, g)
                    if g == LAYER1_AFTER:
                        pe.wait_ge(w1_zero, 1)
                        pe.wait_ge(w1_ready, 1)
                        for m in range(M_TILES):
                            small_layer1(q - 1, m)
                    if g == LAYER2_AFTER:
                        small_layer2(q - 1)
                    if g == LAYER3_AFTER:
                        small_layer3(q - 1)
            for n, (m, h) in enumerate(PIECES):
                if n >= M_TILES:
                    pe.wait_ge(piece_step, PIECE_STEPS * (n - M_TILES) + 2)
                multiply_piece(m, h)
            pe.wait_ge(ones_ready, 1)
            for to, at, width in ((last1, B1_ROW_AT, P), (last2, B2_ROW_AT, P), (last3, B3_ROW_AT, BLOCKS)):
                nc.tensor.matmul(to, params[0:1, at:at + width], ones[:, :], start=True, stop=False)
            for n, (m, h) in enumerate(PIECES):
                last_layer1(n, m, h)
            pe.wait_ge(last_h2_ready, 1)
            nc.tensor.matmul(last2, params[:, W2_AT:W2_AT + P], h2[:, :],
                             start=False, stop=True).then_inc(last2_ready, 1)
            pe.wait_ge(last_h3_ready, 1)
            nc.tensor.matmul(last3, params[:, W3_AT:W3_AT + BLOCKS], h3[:, :],
                             start=False, stop=True).then_inc(last3_ready, 1)


def _lay_out(r_w_features, r_b_features, r_white_to_move, W_in, b_in, W1, b1, W2, b2, W3, b3):
    def stream(x):
        return np.asarray(x).reshape(QUARTERS, Q_ROWS, GROUPS, GROUP, P).transpose(0, 2, 4, 3, 1)

    features = np.stack([stream(r_w_features), stream(r_b_features)], axis=4)
    features = np.ascontiguousarray(features).reshape(QUARTERS * GROUPS, P, GROUP * COLS)
    w_in = np.ascontiguousarray(np.asarray(W_in).reshape(HIDDEN, K_TILES, P).transpose(2, 1, 0))
    small = np.zeros((P, SMALL_COLS), np.float32)
    small[:, W1_AT:B_IN_AT] = np.asarray(W1).reshape(NARROW, MLP_CHUNKS, P).transpose(2, 1, 0).reshape(P, -1)
    small[:, B_IN_AT:B1_AT] = np.asarray(b_in).reshape(M_TILES, P).T
    small[:NARROW, B1_AT] = np.asarray(b1)
    small[0, B1_ROW_AT:B2_ROW_AT] = np.tile(np.asarray(b1), BLOCKS)
    small[0, B2_ROW_AT:B3_ROW_AT] = np.tile(np.asarray(b2), BLOCKS)
    small[0, B3_ROW_AT:SMALL_COLS] = np.asarray(b3)[0]
    for b in range(BLOCKS):
        rows = slice(b * NARROW, (b + 1) * NARROW)
        small[rows, B2_AT] = np.asarray(b2)
        small[b, B3_AT] = np.asarray(b3)[0]
        small[rows, W2_AT + b * NARROW:W2_AT + (b + 1) * NARROW] = np.asarray(W2).T
        small[rows, W3_AT + b] = np.asarray(W3)[0]
    return {
        "features": features,
        "w_in": w_in.reshape(P, K_TILES * HIDDEN),
        "white_to_move": np.ascontiguousarray(r_white_to_move).reshape(1, ROWS),
        "small": small,
    }


def kernel(r_w_features, r_b_features, r_white_to_move, L0_rec_W_in, L0_rec_b_in, L0_rec_W1, L0_rec_b1,
           L0_rec_W2, L0_rec_b2, L0_rec_W3, L0_rec_b3):
    import concourse.bacc as bacc
    from concourse.bass_utils import run_bass_kernel_spmd

    arrays = _lay_out(r_w_features, r_b_features, r_white_to_move, L0_rec_W_in, L0_rec_b_in, L0_rec_W1,
                      L0_rec_b1, L0_rec_W2, L0_rec_b2, L0_rec_W3, L0_rec_b3)
    nc = bacc.Bacc("TRN2", target_bir_lowering=False, num_devices=1)
    args = [nc.dram_tensor(f"{n}_dram", a.shape, mybir.dt.float32, kind="ExternalInput").ap()
            for n, a in arrays.items()]
    out = nc.dram_tensor("scores_dram", (1, ROWS), mybir.dt.float32, kind="ExternalOutput").ap()
    nnue_program(nc, *args, out)
    result = run_bass_kernel_spmd(nc, [{f"{n}_dram": a for n, a in arrays.items()}], core_ids=[0])
    return result.results[0]["scores_dram"].reshape(ROWS, 1)
```
